# Optimizing a Trainium2 kernel written in Bass

```python
import numpy as np
import jax
import jax.numpy as jnp

def _softmax(x, axis=-1):
    return jax.nn.softmax(x, axis=axis)

def _gelu(x):
    return jax.nn.gelu(x, approximate=True)

def _silu(x):
    return jax.nn.silu(x)

def _sigmoid(x):
    return jax.nn.sigmoid(x)

def _layernorm(x, axis=-1, eps=1e-05):
    m = jnp.mean(x, axis=axis, keepdims=True)
    v = jnp.var(x, axis=axis, keepdims=True)
    return (x - m) / jnp.sqrt(v + eps)

def _scatter_add(tgt, idx, src, axis=0):
    return tgt.at[idx].add(src)

def _segment_sum(src, seg, n):
    return jax.ops.segment_sum(src, seg, n)
kernel_name = 'mk_adj_resnorm_d2_adj_r2_c3e8ef'

def setup_inputs(seed: int=0):
    np.random.seed(seed)
    _w = jnp.asarray

    def _rec_inputs():
        import jax
        import jax.numpy as jnp
        _gk = jax.random.key(seed)
        x = -0.000929 + 1 * jax.random.normal(jax.random.fold_in(_gk, 1), (8192, 128), jnp.float32)
        _a = jax.random.bernoulli(jax.random.fold_in(_gk, 2), 0.000244141, (8192, 8192))
        _a = jnp.logical_or(_a, jnp.swapaxes(_a, -1, -2))
        _a = jnp.logical_or(_a, jnp.eye(8192, dtype=bool))
        _af = _a.astype(jnp.float32)
        _af = _af * jax.random.uniform(jax.random.fold_in(_gk, 3), (8192, 8192), jnp.float32, 0.05, 1)
        adj = _af
        return (x, adj)
    x, adj = _rec_inputs()

    def _L0_gnn_setup():
        import jax, jax.numpy as jnp
        import numpy as np
        OVERFLOW_MARGIN = 1e-08
        N, D, OUT = (4096, 128, 128)
        key = jax.random.key(seed)
        k1, k2, k3 = jax.random.split(key, 3)
        values = jax.random.normal(k1, (N, D), dtype=jnp.float32)
        adjacency = jax.random.uniform(k2, (N, N), dtype=jnp.float32)
        W = jax.random.normal(k3, (D, OUT), dtype=jnp.float32) * 0.05
        b = jnp.zeros((OUT,), dtype=jnp.float32)
        return {'values': values, 'adjacency': adjacency, 'W': W, 'b': b}
    _L0_gnn_all = _L0_gnn_setup()
    _L0_gnn_in = {k: v for k, v in _L0_gnn_all.items() if k in ('W', 'b')}
    del _L0_gnn_all

    def _L1_gnn_setup():
        import jax, jax.numpy as jnp
        import numpy as np
        N = 8192
        C = 128
        F = 128
        key = jax.random.key(seed)
        k1, k2, k3, k4 = jax.random.split(key, 4)
        X = jax.random.normal(k1, (N, C), dtype=jnp.float32)
        adj = jax.random.uniform(k2, (N, N), dtype=jnp.float32)
        W = jax.random.normal(k3, (C, F), dtype=jnp.float32) * 0.05
        b = jax.random.normal(k4, (F,), dtype=jnp.float32) * 0.05
        return {'X': X, 'adj': adj, 'W': W, 'b': b}
    _L1_gnn_all = _L1_gnn_setup()
    _L1_gnn_in = {k: v for k, v in _L1_gnn_all.items() if k in ('W', 'b')}
    del _L1_gnn_all
    return {'x': x, 'adj': adj, 'L0_gnn_W': _L0_gnn_in['W'], 'L0_gnn_b': _L0_gnn_in['b'], 'L1_gnn_W': _L1_gnn_in['W'], 'L1_gnn_b': _L1_gnn_in['b']}

def reference(x, adj, L0_gnn_W, L0_gnn_b, L1_gnn_W, L1_gnn_b):
    import jax
    import jax.numpy as jnp

    def _L0_gnn_ref(values, adjacency, W, b):
        import jax, jax.numpy as jnp
        import numpy as np
        OVERFLOW_MARGIN = 1e-08
        N, D, OUT = (4096, 128, 128)
        fc_sc = values @ W + b
        d = jnp.sum(adjacency, axis=1)
        d_inv_sqrt = 1.0 / (jnp.sqrt(d) + OVERFLOW_MARGIN)
        laplacian = adjacency * d_inv_sqrt[:, None] * d_inv_sqrt[None, :]
        return laplacian @ fc_sc

    def _L1_gnn_ref(X, adj, W, b):
        import jax, jax.numpy as jnp
        import numpy as np
        N = 8192
        C = 128
        F = 128
        adj_hat = adj + jnp.eye(adj.shape[0], dtype=adj.dtype)
        d_inv_sqrt = 1.0 / jnp.sqrt(jnp.sum(adj_hat, axis=1))
        adj_norm = adj_hat * d_inv_sqrt[:, None] * d_inv_sqrt[None, :]
        out = adj_norm @ (X @ W) + b
        return jax.nn.relu(out)
    x = _layernorm(x + _L0_gnn_ref(x, adj, L0_gnn_W, L0_gnn_b), axis=-1)
    x = _layernorm(x + _L1_gnn_ref(x, adj, L1_gnn_W, L1_gnn_b), axis=-1)
    return x

_drawn_inputs = setup_inputs


def setup_inputs(seed=0):
    import zlib

    import numpy as np

    out = dict(_drawn_inputs(seed))
    spreads = {'L0_gnn_b': (0.0, 0.1)}
    factors = {}
    for name, (base, spread) in spreads.items():
        noise = np.random.default_rng([zlib.crc32(name.encode()), seed]).standard_normal(out[name].shape)
        drawn = base * np.exp(spread * noise) if base else spread * noise
        out[name] = jnp.asarray(drawn.astype(out[name].dtype))
    for name, factor in factors.items():
        out[name] = (out[name] * factor).astype(out[name].dtype)
    return out
```

```python
from contextlib import ExitStack

import concourse.bass as bass
from concourse import mybir

P = 128
N = 8192
T = 512
Q = T // P
NB = N // T
TILE = Q * T
NEAR = 3
OWN_SLOTS = 10
LENT_SLOTS = 4
BANKS = 6
DEFER = 2

ALU = mybir.AluOpType
ACT = mybir.ActivationFunctionType
AX = mybir.AxisListType
F32 = mybir.dt.float32


def plan():
    loads = [(1, i, j) for i in range(NB) for j in range(NB)]
    loads += [(2, i, j) for i in reversed(range(NB - 1)) for j in reversed(range(i + 1, NB))]
    loads += [(3, i, j) for i in reversed(range(NB)) for j in reversed(range(i + 1))]
    number = {key: n for n, key in enumerate(loads)}

    steps = []

    def product(layer, sweep, i, j):
        steps.append(("product", layer, number[(sweep, i, j)], i, j))

    def scaled(i):
        for k in range(min(NEAR, i) + 1):
            product(0, 1, i - k, i)

    for i in range(NB):
        for j in range(i):
            if j == min(DEFER, i - 1):
                scaled(i - 1)
            product(0, 1, i, j)
        steps += [("features0", i), ("degree", i)]
    scaled(NB - 1)
    for sweep, i, j in loads[NB * NB:]:
        if sweep == 2 and j > i + NEAR:
            product(0, sweep, i, j)
        product(1, sweep, i, j)

    last0 = {}
    last1 = {}
    count = 0
    for s in steps:
        if s[0] == "product":
            (last0 if s[1] == 0 else last1)[s[3]] = count
            if s[1] == 1:
                last1.setdefault(("need", s[4]), count)
            count += 1
    before = {}
    turn0 = -1
    for i in reversed(range(NB)):
        need = last1[("need", i)]
        turn0 = min(max(last0[i] + 2, turn0 + 2), need)
        before.setdefault(turn0, []).append(("turn0", i))
        before.setdefault(min(turn0 + 2, need), []).append(("turn1", i))
        before.setdefault(min(turn0 + 3, need), []).append(("features1", i))
    for i in range(NB):
        before.setdefault(last1[i] + 2, []).append(("turn_out", i))
    out = []
    count = 0
    for s in steps:
        if s[0] == "product":
            out += before.pop(count, [])
            count += 1
        out.append(s)
    for at in sorted(before):
        out += before[at]
    return loads, out


def place(loads, steps):
    last_step = [-1] * len(loads)
    free_at = list(range(len(loads)))
    newest = 0
    unit = 0
    for s in steps:
        if s[0] == "product":
            newest = max(newest, s[2])
            if s[1] == 0 and s[4] < NB - 1:
                newest = max(newest, NB * (s[4] + 1) + 1)
            free_at[s[2]] = newest
            last_step[s[2]] = unit
            unit += 1
    slots = OWN_SLOTS + LENT_SLOTS
    holds = [None] * slots
    slot_of, before = [], []
    for n, (sweep, _, _) in enumerate(loads):
        usable = range(slots if sweep == 1 else OWN_SLOTS)
        s = min(usable, key=lambda s: (-1 if holds[s] is None else free_at[holds[s]], s))
        assert holds[s] is None or free_at[holds[s]] < n
        slot_of.append(s)
        before.append(holds[s])
        holds[s] = n
    return slot_of, before, last_step


def groups(steps):
    first, last, kind_of = {}, {}, []
    unit = 0
    for s in steps:
        if s[0] == "product":
            _, layer, load, i, j = s
            g = (("early0" if j <= i + NEAR else "late0") if layer == 0 else ("right1" if j > i else "left1"), i)
            first.setdefault(g, unit)
            last[g] = unit
            kind_of.append(g)
            unit += 1
    bank, turn = {}, {}
    ends = [-1] * BANKS
    used = [0] * BANKS
    for g in sorted(first, key=lambda g: first[g]):
        b = min(range(BANKS), key=lambda b: ends[b])
        assert ends[b] < first[g]
        bank[g], turn[g] = b, used[b]
        ends[b] = last[g]
        used[b] += 1
    return kind_of, first, last, bank, turn


def gnn_kernel(
    nc: bass.Bass,
    x_rows: bass.AP,
    x_cols: bass.AP,
    adj_tiles: bass.AP,
    w0: bass.AP,
    b0: bass.AP,
    w1: bass.AP,
    b1: bass.AP,
    out: bass.AP,
    x1_rows: bass.AP,
):
    loads, steps = plan()
    slot_of, held_before, last_product = place(loads, steps)
    group_of, first, last, bank_of, bank_turn = groups(steps)
    SLOTS = OWN_SLOTS + LENT_SLOTS

    with ExitStack() as ctx:
        def sb(name, shape):
            return ctx.enter_context(nc.sbuf_tensor(name, shape, F32))

        def sem(name):
            return ctx.enter_context(nc.semaphore(name))

        sums_t = sb("sums_t", [P, NB, T])
        feat0 = sb("feat0", [P, NB * Q, P])
        feat1 = sb("feat1", [P, NB * Q, P])
        own = sb("own", [P, OWN_SLOTS, TILE])
        lent = feat1[:, :, :].rearrange("p (s a) f -> p s (a f)", s=LENT_SLOTS)
        scratch = sb("scratch", [P, 8 * T])
        run = scratch[:, 0:TILE]
        rowsum = scratch[:, 4 * T:5 * T]
        x_t = scratch[:, 5 * T:7 * T].rearrange("p (r n) -> p r n", r=2)
        biased = scratch[:, 7 * T:8 * T].rearrange("p (q f) -> p q f", q=Q)
        y_t = scratch[:, 0:2 * T].rearrange("p (r n) -> p r n", r=2)
        z = scratch[:, 2 * T:3 * T].rearrange("p (q f) -> p q f", q=Q)
        x1_back = scratch[:, 3 * T:5 * T].rearrange("p (r q f) -> p r q f", r=2, q=Q)
        o = scratch[:, 5 * T:7 * T].rearrange("p (r q f) -> p r q f", r=2, q=Q)

        x_in = sb("x_in", [P, 2, Q, P])
        h = sb("h", [P, Q, P])
        x1 = sb("x1", [P, Q, P])
        x1_t = sb("x1_t", [P, T])
        w0_sb = sb("w0_sb", [P, P])
        w1_sb = sb("w1_sb", [P, P])
        b0_sb = sb("b0_sb", [P, P])
        b1_sb = sb("b1_sb", [P, P])
        ident = sb("ident", [P, P])
        ones = sb("ones", [P, 1])
        scale = sb("scale", [P, NB, 2, Q])
        deg = sb("deg", [P, 2, Q])
        root = sb("root", [P, 2, Q])
        inv = sb("inv", [P, 2, Q])
        margin = sb("margin", [P, 2, Q])
        stats = sb("stats", [P, Q, 6])
        moments = sb("moments", [P, Q, 2])
        var = sb("var", [P, Q])
        sdev = sb("sdev", [P, Q])
        rstd = sb("rstd", [P, Q])

        def tile(n, q):
            s = slot_of[n]
            return (own[:, s, q * T:(q + 1) * T] if s < OWN_SLOTS
                    else lent[:, s - OWN_SLOTS, q * T:(q + 1) * T])

        def whole(n):
            s = slot_of[n]
            return own[:, s, :] if s < OWN_SLOTS else lent[:, s - OWN_SLOTS, :]

        acc = [ctx.enter_context(nc.psum_tensor(f"acc{b}", [P, T], F32)) for b in range(BANKS)]
        turned = ctx.enter_context(nc.psum_tensor("turned", [P, T], F32))
        mixed = ctx.enter_context(nc.psum_tensor("mixed", [P, T], F32))
        turned_q = turned[:, :].rearrange("p (q f) -> p q f", q=Q)
        mixed_q = mixed[:, :].rearrange("p (q f) -> p q f", q=Q)

        tile_landed = [sem(f"tile_landed{s}") for s in range(SLOTS)]
        bank_emptied = [sem(f"bank_emptied{b}") for b in range(BANKS)]
        const_landed = sem("const_landed")
        x_t_landed = [sem(f"x_t_landed{r}") for r in range(2)]
        x_landed = [sem(f"x_landed{r}") for r in range(2)]
        x1_back_landed = [sem(f"x1_back_landed{r}") for r in range(2)]
        zeroed = sem("zeroed")
        ident_ready = sem("ident_ready")
        consts_ready = sem("consts_ready")
        products_done = sem("products_done")
        tile_summed = sem("tile_summed")
        row_folded = sem("row_folded")
        mixed0_done = sem("mixed0_done")
        mixed0_used = sem("mixed0_used")
        degree_done = sem("degree_done")
        deg_ready = sem("deg_ready")
        root_ready = sem("root_ready")
        scale_ready = sem("scale_ready")
        feat0_ready = sem("feat0_ready")
        sums0_ready = sem("sums0_ready")
        late_sums0_ready = sem("late_sums0_ready")
        sums1_ready = sem("sums1_ready")
        turn0_done = sem("turn0_done")
        h_ready = sem("h_ready")
        var_ready = sem("var_ready")
        sdev_ready = sem("sdev_ready")
        x1_ready = sem("x1_ready")
        turn1_done = sem("turn1_done")
        x1_t_ready = sem("x1_t_ready")
        mixed1_done = sem("mixed1_done")
        feat1_ready = sem("feat1_ready")
        x1_stored = sem("x1_stored")
        y_t_ready = sem("y_t_ready")
        turn_out_done = sem("turn_out_done")
        z_ready = sem("z_ready")
        out_ready = sem("out_ready")
        out_stored = [sem(f"out_stored{r}") for r in range(2)]
        dve_step = sem("dve_step")

        def nth_up(i):
            return NB - 1 - i

        sums0_rows = [g[1] for g in sorted(last, key=lambda g: last[g]) if g[0] == "early0"]

        landings = []
        seen = [0] * SLOTS
        for n in range(len(loads)):
            seen[slot_of[n]] += 1
            landings.append(seen[slot_of[n]])

        norms = [(s[0], s[1]) for s in steps if s[0] in ("turn0", "turn_out")]
        norm_at = {key: n for n, key in enumerate(norms)}

        block = ctx.enter_context(nc.Block())

        @block.sync
        def _(sp):
            for dst, src in ((w0_sb[:, :], w0), (w1_sb[:, :], w1),
                             (b0_sb[:, :], b0.partition_broadcast(P)), (b1_sb[:, :], b1.partition_broadcast(P))):
                sp.dma_start(dst, src).then_inc(const_landed, 16)
            for n, (sweep, i, j) in enumerate(loads):
                if sweep == 1 and j == 0:
                    if i >= 2:
                        sp.wait_ge(mixed0_done, i - 1)
                    sp.dma_start(x_t[:, i % 2, :], x_cols[:, i * T:(i + 1) * T]).then_inc(x_t_landed[i % 2], 16)
                m = held_before[n]
                if m is not None:
                    if loads[m][0] == 1:
                        sp.wait_ge(tile_summed, m + 1)
                    if last_product[m] >= 0:
                        sp.wait_ge(products_done, last_product[m] + 1)
                sp.dma_start(whole(n), adj_tiles[i, j]).then_inc(tile_landed[slot_of[n]], 16)

        @block.gpsimd
        def _(pool):
            nc.gpsimd.memset(ident[:, :], 0.0).then_inc(zeroed, 1)
            pool.wait_ge(zeroed, 1)
            nc.gpsimd.affine_select(out=ident[:, :], in_=ident[:, :], compare_op=ALU.not_equal, fill=1.0,
                                    base=0, pattern=[[-1, P]], channel_multiplier=1).then_inc(ident_ready, 1)

            def load_x(i):
                r = nth_up(i) % 2
                pool.dma_start(x_in[:, r], x_rows[i]).then_inc(x_landed[r], 16)

            def load_x1(i):
                r = nth_up(i) % 2
                pool.dma_start(x1_back[:, r], x1_rows[i]).then_inc(x1_back_landed[r], 16)

            load_x(NB - 1)
            load_x(NB - 2)
            for i in reversed(range(NB)):
                pool.wait_ge(x1_ready, nth_up(i) + 1)
                pool.dma_start(x1_rows[i], x1[:, :, :]).then_inc(x1_stored, 16)
                if i >= 2:
                    load_x(i - 2)
            pool.wait_ge(x1_stored, 16 * NB)
            load_x1(NB - 1)
            load_x1(NB - 2)
            for i in reversed(range(NB)):
                r = nth_up(i) % 2
                pool.wait_ge(out_ready, nth_up(i) + 1)
                pool.dma_start(out[i], o[:, r]).then_inc(out_stored[r], 16)
                if i >= 2:
                    load_x1(i - 2)
            for r in range(2):
                pool.wait_ge(out_stored[r], 16 * (NB // 2))

        @block.tensor
        def _(pe):
            unit = 0
            for s in steps:
                kind, i = s[0], s[1]

                if kind == "product":
                    _, layer, n, i, j = s
                    g = group_of[unit]
                    if unit == first[g] and bank_turn[g] > 0:
                        pe.wait_ge(bank_emptied[bank_of[g]], bank_turn[g])
                    pe.wait_ge(tile_landed[slot_of[n]], 16 * landings[n])
                    if layer == 0:
                        pe.wait_ge(feat0_ready, j + 1)
                    else:
                        pe.wait_ge(feat1_ready, nth_up(j) + 1)
                    feat = feat0 if layer == 0 else feat1
                    for q in range(Q):
                        mm = nc.tensor.matmul(acc[bank_of[g]][:, :], feat[:, j * Q + q, :], tile(n, q),
                                              start=(unit == first[g] and q == 0),
                                              stop=(unit == last[g] and q == Q - 1))
                    mm.then_inc(products_done, 1)
                    unit += 1

                elif kind == "features0":
                    if i == 0:
                        pe.wait_ge(const_landed, 64)
                    else:
                        pe.wait_ge(mixed0_used, i)
                    pe.wait_ge(x_t_landed[i % 2], 16 * (i // 2 + 1))
                    for q in range(Q):
                        mm = nc.tensor.matmul(mixed_q[:, q, :], x_t[:, i % 2, q * P:(q + 1) * P], w0_sb[:, :],
                                              start=True, stop=True)
                    mm.then_inc(mixed0_done, 1)

                elif kind == "degree":
                    if i == 0:
                        pe.wait_ge(consts_ready, 1)
                    pe.wait_ge(row_folded, i + 1)
                    for q in range(Q):
                        mm = nc.tensor.matmul(turned[:, q:q + 1], rowsum[:, q * P:(q + 1) * P], ones[:, :],
                                              start=True, stop=True)
                    mm.then_inc(degree_done, 1)

                elif kind == "turn0":
                    if i == NB - 1:
                        pe.wait_ge(ident_ready, 1)
                        pe.wait_ge(deg_ready, NB)
                    else:
                        pe.wait_ge(h_ready, nth_up(i))
                    if i < NB - 1 - NEAR:
                        pe.wait_ge(late_sums0_ready, NB - 1 - NEAR - i)
                    else:
                        pe.wait_ge(sums0_ready, sums0_rows.index(i) + 1)
                    for q in range(Q):
                        mm = nc.tensor.transpose(turned_q[:, q, :], sums_t[:, i, q * P:(q + 1) * P], ident[:, :])
                    mm.then_inc(turn0_done, 1)

                elif kind == "turn1":
                    if i == NB - 1:
                        pe.wait_ge(mixed0_used, NB)
                    else:
                        pe.wait_ge(feat1_ready, nth_up(i))
                    pe.wait_ge(x1_ready, nth_up(i) + 1)
                    for q in range(Q):
                        mm = nc.tensor.transpose(mixed_q[:, q, :], x1[:, q, :], ident[:, :])
                    mm.then_inc(turn1_done, 1)

                elif kind == "features1":
                    pe.wait_ge(x1_t_ready, nth_up(i) + 1)
                    for q in range(Q):
                        mm = nc.tensor.matmul(mixed_q[:, q, :], x1_t[:, q * P:(q + 1) * P], w1_sb[:, :],
                                              start=True, stop=True)
                    mm.then_inc(mixed1_done, 1)

                elif kind == "turn_out":
                    if i == NB - 1:
                        pe.wait_ge(h_ready, NB)
                    else:
                        pe.wait_ge(z_ready, nth_up(i))
                    pe.wait_ge(y_t_ready, nth_up(i) + 1)
                    for q in range(Q):
                        mm = nc.tensor.transpose(turned_q[:, q, :], y_t[:, nth_up(i) % 2, q * P:(q + 1) * P],
                                                 ident[:, :])
                    mm.then_inc(turn_out_done, 1)

        @block.scalar
        def _(act):
            def root_of_variance(key):
                act.wait_ge(var_ready, norm_at[key] + 1)
                nc.scalar.activation(sdev[:, :], var[:, :], ACT.Sqrt).then_inc(sdev_ready, 1)

            unit = 0
            for s in steps:
                kind, i = s[0], s[1]
                if kind == "degree":
                    act.wait_ge(deg_ready, i + 1)
                    nc.scalar.activation(root[:, :, :], deg[:, :, :], ACT.Sqrt).then_inc(root_ready, 1)
                    act.wait_ge(scale_ready, i + 1)
                    act.wait_ge(mixed0_used, i + 1)
                    for q in range(Q):
                        ins = nc.scalar.activation(feat0[:, i * Q + q, :], biased[:, q, :], ACT.Copy,
                                                   scale=scale[:, i, 0, q:q + 1])
                    ins.then_inc(feat0_ready, 1)
                elif kind == "product":
                    g = group_of[unit]
                    if unit == last[g] and g[0] in ("early0", "right1"):
                        act.wait_ge(products_done, unit + 1)
                        nc.scalar.copy(sums_t[:, g[1], :], acc[bank_of[g]][:, :]).then_inc(bank_emptied[bank_of[g]], 1)
                        act.wait_ge(bank_emptied[bank_of[g]], bank_turn[g] + 1)
                        act.sem_inc(sums0_ready if g[0] == "early0" else sums1_ready, 1)
                    unit += 1
                elif kind == "turn0":
                    root_of_variance((kind, i))
                elif kind == "turn1":
                    act.wait_ge(turn1_done, nth_up(i) + 1)
                    nc.scalar.copy(x1_t[:, :], mixed[:, :]).then_inc(x1_t_ready, 1)
                elif kind == "features1":
                    act.wait_ge(mixed1_done, nth_up(i) + 1)
                    for q in range(Q):
                        ins = nc.scalar.activation(feat1[:, i * Q + q, :], mixed_q[:, q, :], ACT.Copy,
                                                   scale=scale[:, i, 1, q:q + 1])
                    ins.then_inc(feat1_ready, 1)
                elif kind == "turn_out":
                    root_of_variance((kind, i))

        @block.vector
        def _(dve):
            taken = [0]

            def then(ins):
                taken[0] += 1
                ins.then_inc(dve_step, 1)
                dve.wait_ge(dve_step, taken[0])

            nc.vector.memset(margin[:, 1, :], 0.0)
            nc.vector.memset(margin[:, 0, :], 1e-8)
            nc.vector.memset(ones[:, :], 1.0).then_inc(consts_ready, 1)
            dve.wait_ge(consts_ready, 1)

            def refine(dst, square, guess):
                then(nc.vector.tensor_scalar(guess, guess, 1e-30, None, ALU.max))
                then(nc.vector.reciprocal(dst, guess))
                then(nc.vector.tensor_tensor(dst, dst, square, ALU.mult))
                then(nc.vector.tensor_tensor(dst, dst, guess, ALU.add))

            def take_degree(i):
                dve.wait_ge(degree_done, i + 1)
                if i > 0:
                    dve.wait_ge(root_ready, i)
                    dve.wait_ge(scale_ready, i)
                nc.vector.tensor_copy(deg[:, 0, :], turned[:, 0:Q])
                nc.vector.tensor_scalar(deg[:, 1, :], turned[:, 0:Q], 1.0, None, ALU.add).then_inc(deg_ready, 1)

            def make_scale(i):
                dve.wait_ge(mixed0_done, i + 1)
                if i > 0:
                    dve.wait_ge(feat0_ready, i)
                for q in range(Q):
                    ins = nc.vector.tensor_tensor(biased[:, q, :], mixed_q[:, q, :], b0_sb[:, :], ALU.add)
                ins.then_inc(mixed0_used, 1)
                dve.wait_ge(root_ready, i + 1)
                refine(inv[:, :, :], deg[:, :, :], root[:, :, :])
                then(nc.vector.scalar_tensor_tensor(out=inv[:, :, :], in0=inv[:, :, :], scalar=0.5,
                                                    in1=margin[:, :, :], op0=ALU.mult, op1=ALU.add))
                nc.vector.reciprocal(scale[:, i, :, :], inv[:, :, :]).then_inc(scale_ready, 1)

            def h_normalised(n):
                kind, i = norms[n]
                dve.wait_ge(x1_ready if kind == "turn0" else out_ready, nth_up(i) + 1)

            def normalise(key, dst, done):
                for q in range(Q):
                    ins = nc.vector.bn_stats(stats[:, q, :], h[:, q, :])
                then(ins)
                for q in range(Q):
                    ins = nc.vector.bn_aggr(moments[:, q, :], stats[:, q, :])
                then(ins)
                nc.vector.tensor_scalar(var[:, :], moments[:, :, 1], 1e-5, None, ALU.add).then_inc(var_ready, 1)
                dve.wait_ge(sdev_ready, norm_at[key] + 1)
                refine(rstd[:, :], var[:, :], sdev[:, :])
                then(nc.vector.tensor_scalar(rstd[:, :], rstd[:, :], 0.5, None, ALU.mult))
                then(nc.vector.reciprocal(rstd[:, :], rstd[:, :]))
                for q in range(Q):
                    ins = nc.vector.tensor_scalar(dst[:, q, :], h[:, q, :], moments[:, q, 0:1], rstd[:, q:q + 1],
                                                  ALU.subtract, ALU.mult)
                ins.then_inc(done, 1)

            for n in range(NB * NB):
                i, j = n // NB, n % NB
                dve.wait_ge(tile_landed[slot_of[n]], 16 * landings[n])
                if j == 0:
                    if i > 0:
                        dve.wait_ge(row_folded, i)
                    ins = nc.vector.tensor_copy(run, whole(n))
                else:
                    dve.wait_ge(tile_summed, n)
                    ins = nc.vector.tensor_tensor(run, run, whole(n), ALU.add)
                ins.then_inc(tile_summed, 1)
                if i > 0 and j == 0:
                    take_degree(i - 1)
                if i > 0 and j == 1:
                    make_scale(i - 1)
                if j == NB - 1:
                    dve.wait_ge(tile_summed, n + 1)
                    if i > 0:
                        dve.wait_ge(degree_done, i)
                    nc.vector.tensor_reduce(rowsum, run.rearrange("p (q n) -> p n q", q=Q), AX.X,
                                            ALU.add).then_inc(row_folded, 1)
            take_degree(NB - 1)
            make_scale(NB - 1)

            unit = 0
            for s in steps:
                kind, i = s[0], s[1]
                if kind == "product":
                    g = group_of[unit]
                    if unit == last[g] and g[0] == "late0":
                        dve.wait_ge(products_done, unit + 1)
                        dve.wait_ge(sums0_ready, sums0_rows.index(g[1]) + 1)
                        nc.vector.tensor_tensor(sums_t[:, g[1], :], sums_t[:, g[1], :], acc[bank_of[g]][:, :],
                                                ALU.add).then_inc(bank_emptied[bank_of[g]], 1)
                        dve.wait_ge(bank_emptied[bank_of[g]], bank_turn[g] + 1)
                        dve.sem_inc(late_sums0_ready, 1)
                    if unit == last[g] and g[0] == "left1":
                        r = nth_up(g[1]) % 2
                        dve.wait_ge(products_done, unit + 1)
                        if nth_up(g[1]) >= 2:
                            dve.wait_ge(turn_out_done, nth_up(g[1]) - 1)
                        if g[1] == NB - 1:
                            ins = nc.vector.tensor_copy(y_t[:, r, :], acc[bank_of[g]][:, :])
                        else:
                            dve.wait_ge(sums1_ready, nth_up(g[1]))
                            ins = nc.vector.tensor_tensor(y_t[:, r, :], acc[bank_of[g]][:, :], sums_t[:, g[1], :],
                                                          ALU.add)
                        ins.then_inc(bank_emptied[bank_of[g]], 1)
                        dve.wait_ge(bank_emptied[bank_of[g]], bank_turn[g] + 1)
                        dve.sem_inc(y_t_ready, 1)
                    unit += 1
                elif kind == "turn0":
                    dve.wait_ge(turn0_done, nth_up(i) + 1)
                    dve.wait_ge(x_landed[nth_up(i) % 2], 16 * (nth_up(i) // 2 + 1))
                    if norm_at[(kind, i)] > 0:
                        h_normalised(norm_at[(kind, i)] - 1)
                    for q in range(Q):
                        ins = nc.vector.scalar_tensor_tensor(
                            out=h[:, q, :], in0=turned_q[:, q, :], scalar=scale[:, i, 0, q:q + 1],
                            in1=x_in[:, nth_up(i) % 2, q, :], op0=ALU.mult, op1=ALU.add)
                    ins.then_inc(h_ready, 1)
                    dve.wait_ge(h_ready, nth_up(i) + 1)
                    if i < NB - 1:
                        dve.wait_ge(turn1_done, nth_up(i))
                        dve.wait_ge(x1_stored, 16 * nth_up(i))
                    normalise((kind, i), x1, x1_ready)
                elif kind == "turn_out":
                    r = nth_up(i) % 2
                    dve.wait_ge(turn_out_done, nth_up(i) + 1)
                    dve.wait_ge(feat1_ready, nth_up(i) + 1)
                    nc.vector.tensor_tensor(z, turned_q[:, :, :], feat1[:, i * Q:(i + 1) * Q, :],
                                            ALU.add).then_inc(z_ready, 1)
                    dve.wait_ge(z_ready, nth_up(i) + 1)
                    for q in range(Q):
                        ins = nc.vector.scalar_tensor_tensor(
                            out=z[:, q, :], in0=z[:, q, :], scalar=scale[:, i, 1, q:q + 1],
                            in1=b1_sb[:, :], op0=ALU.mult, op1=ALU.add)
                    then(ins)
                    dve.wait_ge(x1_back_landed[r], 16 * (nth_up(i) // 2 + 1))
                    h_normalised(norm_at[(kind, i)] - 1)
                    then(nc.vector.scalar_tensor_tensor(out=h[:, :, :], in0=z, scalar=0.0,
                                                        in1=x1_back[:, r], op0=ALU.max, op1=ALU.add))
                    if nth_up(i) >= 2:
                        dve.wait_ge(out_stored[r], 16 * (nth_up(i) // 2))
                    normalise((kind, i), o[:, r], out_ready)


def kernel(x, adj, L0_gnn_W, L0_gnn_b, L1_gnn_W, L1_gnn_b):
    import numpy as _np
    import concourse.bacc as _bacc
    from concourse.bass_utils import run_bass_kernel_spmd as _run

    arrays = {
        "x_rows": _np.ascontiguousarray(_np.asarray(x).reshape(NB, Q, P, P).transpose(0, 2, 1, 3)),
        "x_cols": _np.ascontiguousarray(_np.asarray(x).T),
        "adj_tiles": _np.ascontiguousarray(
            _np.asarray(adj).reshape(NB, T, NB, Q, P).transpose(0, 2, 4, 3, 1)).reshape(NB, NB, P, TILE),
        "w0": _np.ascontiguousarray(L0_gnn_W),
        "b0": _np.ascontiguousarray(L0_gnn_b),
        "w1": _np.ascontiguousarray(L1_gnn_W),
        "b1": _np.ascontiguousarray(L1_gnn_b),
    }
    nc = _bacc.Bacc("TRN2", target_bir_lowering=False, num_devices=1)
    args = [nc.dram_tensor(name, a.shape, F32, kind="ExternalInput").ap() for name, a in arrays.items()]
    args.append(nc.dram_tensor("out_rows", (NB, P, Q, P), F32, kind="ExternalOutput").ap())
    args.append(nc.dram_tensor("x1_rows", (NB, P, Q, P), F32, kind="Internal").ap())
    gnn_kernel(nc, *args)
    r = _run(nc, [arrays], core_ids=[0])
    got = r.results[0]["out_rows"]
    return _np.ascontiguousarray(got.transpose(0, 2, 1, 3)).reshape(N, P)
```

```python
from contextlib import ExitStack

import concourse.bass as bass
from concourse import mybir

P = 128
N = 8192
T = 512
Q = T // P
NB = N // T
TILE = Q * T
HALF = TILE // 2
HQ = Q // 2
NEAR = [1] * NB
PE_SUMS = [min(i, 8) for i in range(NB)]
OWN_SLOTS = 3
LENT_SLOTS = 6
RING = 4
MORE = 2
AHEAD = {1: 1, 2: 0, 3: 1}
BANKS = 5
SCALE_LAG = 1
SPLIT_LAG = 2
TURN_EVERY, TURN1_LAG, FEATURES1_LAG = 2, 3, 1
ROWS3 = [r for k in range(NB // 2) for r in (NB - 1 - k, k)]

ALU = mybir.AluOpType
ACT = mybir.ActivationFunctionType
AX = mybir.AxisListType
F32 = mybir.dt.float32
F32R = mybir.dt.float32r


def held(j):
    return min(j, NEAR[j])


def early(i, j):
    return i + held(j) >= j


def pe_sums(i, j):
    return j < PE_SUMS[i]


def row_order(i):
    left = list(range(i))
    wait = [j for j in range(i, NB) if early(i, j)]
    far = [j for j in range(i, NB) if not early(i, j)]
    spread = sorted([((k + 0.5) / len(left), j) for k, j in enumerate(left)] +
                    [((k + 0.5) / len(far), j) for k, j in enumerate(far)])
    return [j for _, j in spread] + wait


def up(i):
    return NB - 1 - i


class Plan:

    def __init__(self):
        self.loads = [(1, i, j) for i in range(NB) for j in row_order(i)]
        self.loads += [(2, i, j) for i in reversed(range(NB - 1)) for j in reversed(range(i + 1, NB))]
        self.loads += [(3, i, j) for i in ROWS3 for j in reversed(range(i + 1))]
        number = {key: n for n, key in enumerate(self.loads)}
        self.takes, self.pe_before = [], {}

        needs, order = [], []

        def take(sweep, i, j, layers, scaled=False):
            n = number[(sweep, i, j)]
            late = NB * (j + 1) + SCALE_LAG
            needs.append(max(n, min(late, NB * NB - 1) if scaled else 0, needs[-1] if needs else 0))
            order.append(max(n, late if scaled else 0, order[-1] if order else 0))
            self.takes.append((n, i, j, layers))

        def scaled_takes(i):
            for k in range(held(i) + 1):
                take(1, i - k, i, (0,), scaled=True)

        for i in range(NB):
            done = i == 0
            for j in range(i):
                if not done and (number[(1, i, j)] > i * NB + SCALE_LAG or j == i - 1):
                    scaled_takes(i - 1)
                    done = True
                take(1, i, j, (0,))
            self.pe_before.setdefault(len(self.takes), []).extend([("features0", i), ("degree", i)])
        scaled_takes(NB - 1)
        for sweep, i, j in self.loads[NB * NB:]:
            take(sweep, i, j, (0, 1) if sweep == 2 and not early(i, j) else (1,))
        self.end = len(self.takes)
        self.needs = needs

        self.group = []
        first, self.last = {}, {}
        for u, (n, i, j, layers) in enumerate(self.takes):
            of = {}
            for layer in layers:
                kind = ("early0" if early(i, j) else "late0") if layer == 0 else ("right1" if j > i else "left1")
                g = of[layer] = (kind, i)
                first.setdefault(g, u)
                self.last[g] = u
            self.group.append(of)
        self.first = first

        feature_needed = {}
        for u, (_, i, j, layers) in enumerate(self.takes):
            if 1 in layers:
                feature_needed.setdefault(j, u)
        self.late_rows = [i for i in reversed(range(NB)) if ("late0", i) in first]
        self.turn0, self.turn1, self.features1 = {}, {}, {}
        before = -TURN_EVERY
        for i in reversed(range(NB)):
            end = self.last[("late0", i) if i in self.late_rows else ("early0", i)]
            need = feature_needed[i]
            before = self.turn0[i] = min(max(end + 2, before + TURN_EVERY), need)
            self.turn1[i] = min(before + TURN1_LAG, need)
            self.features1[i] = min(self.turn1[i] + FEATURES1_LAG, need)
        self.empty = {g: u + 1 for g, u in self.last.items()}
        for i in range(NB):
            if i not in self.late_rows:
                self.empty[("early0", i)] = max(self.turn0[i] - 1, self.last[("early0", i)] + 1)
        self.turn_out = {}
        for m, i in enumerate(ROWS3):
            g = ("left1", i)
            if m >= 2:
                self.empty[g] = max(self.empty[g], self.turn_out[ROWS3[m - 2]])
            self.turn_out[i] = self.empty[g] + 1
            if m >= 1:
                self.turn_out[i] = max(self.turn_out[i], self.turn_out[ROWS3[m - 1]] + 2)
        for table, kind in ((self.turn0, "turn0"), (self.turn1, "turn1"), (self.features1, "features1")):
            for i in reversed(range(NB)):
                self.pe_before.setdefault(min(table[i], self.end), []).append((kind, i))
        for i in ROWS3:
            self.pe_before.setdefault(min(self.turn_out[i], self.end), []).append(("turn_out", i))

        self.bank, self.bank_turn = {}, {}
        ends, used = [-1] * BANKS, [0] * BANKS
        for g in sorted(first, key=lambda g: first[g]):
            b = min(range(BANKS), key=lambda b: ends[b])
            assert ends[b] <= first[g], (g, ends)
            self.bank[g], self.bank_turn[g] = b, used[b]
            ends[b] = self.empty[g]
            used[b] += 1

        lo_order = []
        for u, (n, i, j, layers) in enumerate(self.takes):
            key = (order[u] + SPLIT_LAG, 0.3)
            if self.loads[n][0] == 1 and j < i:
                key = min(key, (NB * (i + 1) - 1, 0.3))
            lo_order.append(max(key, lo_order[-1] if lo_order else key))

        self.take_of = {n: u for u, (n, _, _, _) in enumerate(self.takes)}
        last_late0 = max(self.last[g] for g in self.last if g[0] == "late0")
        self.lent_again = last_late0
        holds = [None] * (OWN_SLOTS + 2 * LENT_SLOTS)
        self.slot, self.held_before = [], []
        for n, (sweep, i, j) in enumerate(self.loads):
            usable = list(range(OWN_SLOTS))
            if sweep == 1:
                usable += range(OWN_SLOTS, OWN_SLOTS + LENT_SLOTS)
            if sweep == 3:
                usable += range(OWN_SLOTS + LENT_SLOTS, OWN_SLOTS + 2 * LENT_SLOTS)

            def free_at(s):
                m = holds[s]
                if m is None:
                    return -1 if s < OWN_SLOTS + LENT_SLOTS else needs[last_late0]
                if m not in self.take_of:
                    return m
                u = self.take_of[m]
                return max(needs[u], min(lo_order[u][0], NB * NB - 1)) if self.loads[m][0] == 1 else needs[u]

            s = min(usable, key=lambda s: (free_at(s), s))
            assert free_at(s) < n, (n, s, free_at(s))
            self.slot.append(s)
            self.held_before.append(holds[s])
            holds[s] = n

        self.buffer, self.half_before, where = [], [], {}
        for u, (n, _, _, _) in enumerate(self.takes):
            sweep = self.loads[n][0]
            ring = [(0, b) for b in range(RING)] + ([(sweep, b) for b in range(MORE)] if sweep != 2 else [])
            for half in range(2):
                b = min(ring, key=lambda b: where.get(b, -1 if b[0] != 3 else 2 * last_late0 + 1))
                self.buffer.append(b)
                self.half_before.append(where.get(b, -1 if b[0] != 3 else 2 * last_late0 + 1))
                where[b] = 2 * u + half

        self.landings, seen = [], [0] * len(holds)
        self.summed, total = [], 0
        for n, (sweep, i, j) in enumerate(self.loads):
            seen[self.slot[n]] += 1
            self.landings.append(seen[self.slot[n]])
            total += sweep == 1 and not pe_sums(i, j)
            self.summed.append(total)

        inf = float("inf")

        def ahead(k, sub):
            return k + AHEAD[self.loads[self.takes[k][0]][0]] if sub and k < self.end else k

        def hi_key(k, sub):
            k = ahead(k, sub)
            return (order[k], 0.25, k, sub) if k < self.end else (inf, 0, k, sub)

        def lo_key(k, sub):
            k = ahead(k, sub)
            return (*lo_order[k], k, sub) if k < self.end else (inf, 0, k, sub)

        act, dve, pool = [], [], []
        for u in range(self.end):
            act.append((hi_key(u, 0), "high", u))
            dve.append((lo_key(u, 0), "low", u))
        for n in range(NB * NB):
            if not pe_sums(*self.loads[n][1:]):
                dve.append(((n, 0, 0, 0), "sum", n))
        for i in range(NB):
            row = NB * (i + 1)
            dve.append(((row - 1, 0.4, 0, 0), "fold", i))
            dve.append(((row, 0.1, 0, 0), "take_degree", i))
            act.append(((row, 0.15, 0, 0), "root", i))
            dve.append(((row + SCALE_LAG, 0.2, 0, 0), "make_scale", i))
            act.append(((row + SCALE_LAG, 0.22, 0, 0), "features0_high", i))
            dve.append(((row + SCALE_LAG + SPLIT_LAG, 0.28, 0, 0), "features0_low", i))
        for g in self.last:
            k = self.empty[g]
            (act if g[0] in ("early0", "right1") else dve).append(
                ((hi_key if g[0] in ("early0", "right1") else lo_key)(k, 1), "empty_" + g[0], g[1]))
            if g[0] == "right1" or (g[0] == "early0" and g[1] in self.late_rows):
                pool.append(((k, 2, 0), "store_" + g[0], g[1]))
        for i in reversed(range(NB)):
            k0, k1, k2 = self.turn0[i], self.turn1[i], self.features1[i]
            split = min(k0 + 1, k1)
            dve.append((lo_key(k0, 3), "add_x", i))
            act.append((hi_key(split, 4), "root_x1", i))
            dve.append((lo_key(split, 5), "make_x1", i))
            act.append((hi_key(k1, 6), "x1_columns", i))
            act.append((hi_key(k2, 7), "features1_high", i))
            dve.append((lo_key(k2, 8), "features1_low", i))
            pool.append(((split, 5, 0), "store_x1", i))
            free = self.turn0[i + 2] if i + 2 < NB else self.first[("early0", NB - 1)]
            if i + 2 >= NB:
                free = self.last[("early0", NB - 1)] - 1
            pool.append(((max(k0 - 5, free), 9, up(i)), "load_x", i))
        for m, i in enumerate(ROWS3):
            k = self.turn_out[i]
            dve.append((lo_key(k, 3), "add_x1", i))
            act.append((hi_key(k + 1, 4), "root_out", i))
            dve.append((lo_key(k + 1, 5), "make_out", i))
            pool.append(((k + 1, 5, 0), "store_out", i))
            free = self.turn_out[ROWS3[m - 2]] if m >= 2 else self.features1[0]
            pool.append(((max(self.empty[("left1", i)] - 6, free), 9, m), "load_x1", i))
        self.act = [e[1:] for e in sorted(act)]
        self.dve = [e[1:] for e in sorted(dve)]
        self.pool = [e[1:] for e in sorted(pool)]

    def nth(self, engine, kinds):
        return {(kind, i): m for m, (kind, i) in enumerate(e for e in engine if e[0] in kinds)}


def gnn_kernel(
    nc: bass.Bass,
    x_rows: bass.AP,
    x_cols: bass.AP,
    adj_tiles: bass.AP,
    w0: bass.AP,
    b0: bass.AP,
    w1: bass.AP,
    b1: bass.AP,
    out: bass.AP,
    x1_rows: bass.AP,
    sums_rows: bass.AP,
):
    plan = Plan()
    loads, takes, end = plan.loads, plan.takes, plan.end
    SLOTS = OWN_SLOTS + 2 * LENT_SLOTS

    with ExitStack() as ctx:
        def sem(name):
            return ctx.enter_context(nc.semaphore(name))

        top = [-(-nc.sbuf_base // 64) * 64]

        def at(offset, name, shape, dtype=F32):
            return nc.alloc_sbuf_tensor_at(name, shape, dtype, offset=offset)

        def take_bytes(nbytes):
            offset = top[0]
            top[0] += -(-nbytes // 64) * 64
            return offset

        def put(name, shape, dtype=F32):
            nbytes = 4
            for d in shape[1:]:
                nbytes *= d
            return at(take_bytes(nbytes), name, shape, dtype)

        feats = NB * Q * P * 4
        feat0_at, feat1_at = take_bytes(2 * feats), take_bytes(2 * feats)
        feat_high = [at(o, f"feat{k}_high", [P, NB * Q, P], F32R) for k, o in enumerate((feat0_at, feat1_at))]
        feat_low = [at(o + feats, f"feat{k}_low", [P, NB * Q, P], F32R) for k, o in enumerate((feat0_at, feat1_at))]
        own = put("own", [P, OWN_SLOTS, TILE])
        lent1 = at(feat1_at, "lent1", [P, LENT_SLOTS, TILE])
        lent3 = at(feat0_at, "lent3", [P, LENT_SLOTS, TILE])
        high_ring = {0: put("high0", [P, RING, HALF], F32R)}
        low_ring = {0: put("low0", [P, RING, HALF], F32R)}
        for sweep, offset in ((1, feat1_at), (3, feat0_at)):
            offset += LENT_SLOTS * TILE * 4
            high_ring[sweep] = at(offset, f"high{sweep}", [P, MORE, HALF], F32R)
            low_ring[sweep] = at(offset + MORE * HALF * 4, f"low{sweep}", [P, MORE, HALF], F32R)
        stage_at_byte = take_bytes(2 * T * 4)
        stage = at(stage_at_byte, "stage", [P, 2, T])
        o = at(stage_at_byte, "o", [P, 2, Q, P])
        scratch = take_bytes(8 * T * 4)
        run = at(scratch, "run", [P, TILE])
        rowsum = at(scratch + 16 * T, "rowsum", [P, T])
        x_t = at(scratch + 20 * T, "x_t", [P, 2, T])
        biased = at(scratch + 28 * T, "biased", [P, Q, P])
        x_in = at(scratch, "x_in", [P, 2, Q, P])
        sums_in = at(scratch + 8 * T, "sums_in", [P, 2, T])
        h = at(scratch + 16 * T, "h", [P, Q, P])
        x1 = at(scratch + 20 * T, "x1", [P, Q, P])
        z = at(scratch + 20 * T, "z", [P, Q, P])
        x1_t = at(scratch + 24 * T, "x1_t", [P, T])
        y_t = at(scratch + 24 * T, "y_t", [P, 2, T])

        w_sb = put("w_sb", [P, P])
        b_sb = put("b_sb", [P, P])
        ident = put("ident", [P, P])
        ident_r = put("ident_r", [P, P], F32R)
        ones = put("ones", [P, 1])
        ones_r = put("ones_r", [P, P], F32R)
        scale = put("scale", [P, NB, 2, Q])
        deg = put("deg", [P, 2, Q])
        root = put("root", [P, 2, Q])
        inv = put("inv", [P, 2, Q])
        margin = put("margin", [P, 2, Q])
        stats = put("stats", [P, Q, 6])
        moments = put("moments", [P, Q, 2])
        var = put("var", [P, Q])
        sdev = put("sdev", [P, Q])
        rstd = put("rstd", [P, Q])

        def raw(n):
            s = plan.slot[n]
            if s < OWN_SLOTS:
                return own[:, s, :]
            s -= OWN_SLOTS
            return lent1[:, s, :] if s < LENT_SLOTS else lent3[:, s - LENT_SLOTS, :]

        def high(m):
            ring, b = plan.buffer[m]
            return high_ring[ring][:, b, :]

        def low(m):
            ring, b = plan.buffer[m]
            return low_ring[ring][:, b, :]

        acc = [ctx.enter_context(nc.psum_tensor(f"acc{b}", [P, T], F32)) for b in range(BANKS)]
        part = ctx.enter_context(nc.psum_tensor("part", [P, T], F32))
        turned = ctx.enter_context(nc.psum_tensor("turned", [P, T], F32))
        mixed = ctx.enter_context(nc.psum_tensor("mixed", [P, T], F32))
        turned_q = turned[:, :].rearrange("p (q f) -> p q f", q=Q)
        mixed_q = mixed[:, :].rearrange("p (q f) -> p q f", q=Q)

        tile_landed = [sem(f"tile_landed{s}") for s in range(SLOTS)]
        bank_emptied = [sem(f"bank_emptied{b}") for b in range(BANKS)]
        const_landed = sem("const_landed")
        const1_landed = sem("const1_landed")
        x_t_landed = [sem(f"x_t_landed{r}") for r in range(2)]
        x_landed = [sem(f"x_landed{r}") for r in range(2)]
        zeroed = sem("zeroed")
        ident_ready = sem("ident_ready")
        consts_ready = sem("consts_ready")
        high_ready = sem("high_ready")
        low_ready = sem("low_ready")
        halves_used = sem("halves_used")
        tile_summed = sem("tile_summed")
        row_folded = sem("row_folded")
        mixed0_done = sem("mixed0_done")
        mixed0_used = sem("mixed0_used")
        degree_done = sem("degree_done")
        deg_ready = sem("deg_ready")
        root_ready = sem("root_ready")
        scale_ready = sem("scale_ready")
        feat0_high_ready = sem("feat0_high_ready")
        feat0_ready = sem("feat0_ready")
        staged = sem("staged")
        sums_stored = [sem(f"sums_stored{r}") for r in range(2)]
        sums0_ready = sem("sums0_ready")
        turn0_done = sem("turn0_done")
        h_ready = sem("h_ready")
        var_ready = sem("var_ready")
        sdev_ready = sem("sdev_ready")
        x1_ready = sem("x1_ready")
        turn1_done = sem("turn1_done")
        x1_t_ready = sem("x1_t_ready")
        mixed1_done = sem("mixed1_done")
        feat1_high_ready = sem("feat1_high_ready")
        feat1_ready = sem("feat1_ready")
        x1_stored = sem("x1_stored")
        y_t_ready = sem("y_t_ready")
        turn_out_done = sem("turn_out_done")
        z_ready = sem("z_ready")
        out_ready = sem("out_ready")
        out_stored = [sem(f"out_stored{r}") for r in range(2)]
        dve_step = sem("dve_step")

        norm = plan.nth(plan.dve, ("make_x1", "make_out"))
        stage_at = plan.nth([e for e in plan.act if e[0] == "empty_right1" or
                             (e[0] == "empty_early0" and e[1] in plan.late_rows)],
                            ("empty_early0", "empty_right1"))
        third = {i: m for m, i in enumerate(ROWS3)}

        def ring_of_x(i):
            r = up(i) % 2
            loaded = sum(16 * (2 if k in plan.late_rows else 1) for k in range(i, NB) if up(k) % 2 == r)
            return r, loaded

        def ring_of_x1(i):
            r = third[i] % 2
            before = ring_of_x(0 if up(0) % 2 == r else 1)[1]
            loaded = sum(16 * (2 if k != NB - 1 else 1) for k in ROWS3[:third[i] + 1] if third[k] % 2 == r)
            return r, before + loaded

        block = ctx.enter_context(nc.Block())

        @block.sync
        def _(sp):
            sp.dma_start(w_sb[:, :], w0).then_inc(const_landed, 16)
            sp.dma_start(b_sb[:, :], b0.partition_broadcast(P)).then_inc(const_landed, 16)
            for n, (sweep, i, j) in enumerate(loads):
                if sweep == 1 and n % NB == 0:
                    if i >= 2:
                        sp.wait_ge(mixed0_done, i - 1)
                    sp.dma_start(x_t[:, i % 2, :], x_cols[:, i * T:(i + 1) * T]).then_inc(x_t_landed[i % 2], 16)
                m = plan.held_before[n]
                if m is not None:
                    if loads[m][0] == 1 and not pe_sums(*loads[m][1:]):
                        sp.wait_ge(tile_summed, plan.summed[m])
                    if m in plan.take_of:
                        sp.wait_ge(low_ready, 2 * plan.take_of[m] + 2)
                elif plan.slot[n] >= OWN_SLOTS + LENT_SLOTS:
                    sp.wait_ge(halves_used, 2 * plan.lent_again + 2)
                sp.dma_start(raw(n), adj_tiles[i, j]).then_inc(tile_landed[plan.slot[n]], 16)

        @block.gpsimd
        def _(pool):
            nc.gpsimd.memset(ident[:, :], 0.0).then_inc(zeroed, 1)
            pool.wait_ge(zeroed, 1)
            nc.gpsimd.affine_select(out=ident[:, :], in_=ident[:, :], compare_op=ALU.not_equal, fill=1.0,
                                    base=0, pattern=[[-1, P]], channel_multiplier=1).then_inc(ident_ready, 1)
            pool.wait_ge(ident_ready, 1)
            nc.gpsimd.tensor_copy(ident_r[:, :], ident[:, :]).then_inc(ident_ready, 1)

            def stored(layer, i):
                m = stage_at[("empty_right1" if layer else "empty_early0", i)]
                pool.wait_ge(sums_stored[m % 2], 16 * (m // 2 + 1))

            for kind, i in plan.pool:
                if kind in ("store_early0", "store_right1"):
                    m = stage_at[(kind.replace("store", "empty"), i)]
                    pool.wait_ge(staged, m + 1)
                    pool.dma_start(sums_rows[int(kind == "store_right1"), i], stage[:, m % 2, :])\
                        .then_inc(sums_stored[m % 2], 16)
                elif kind == "load_x":
                    r, _ = ring_of_x(i)
                    if i >= NB - 2:
                        pool.wait_ge(scale_ready, NB)
                        if i == NB - 1:
                            pool.dma_start(w_sb[:, :], w1).then_inc(const1_landed, 16)
                            pool.dma_start(b_sb[:, :], b1.partition_broadcast(P)).then_inc(const1_landed, 16)
                    else:
                        pool.wait_ge(h_ready, up(i) - 1)
                    pool.dma_start(x_in[:, r], x_rows[i]).then_inc(x_landed[r], 16)
                    if i in plan.late_rows:
                        stored(0, i)
                        pool.wait_ge(turn0_done, up(i) - 1)
                        pool.dma_start(sums_in[:, r, :], sums_rows[0, i]).then_inc(x_landed[r], 16)
                elif kind == "store_x1":
                    pool.wait_ge(x1_ready, up(i) + 1)
                    pool.dma_start(x1_rows[i], x1[:, :, :]).then_inc(x1_stored, 16)
                elif kind == "load_x1":
                    r, _ = ring_of_x1(i)
                    m = third[i]
                    pool.wait_ge(x1_stored, 16 * NB)
                    pool.wait_ge(h_ready, NB)
                    if m >= 2:
                        pool.wait_ge(z_ready, 2 * (m - 1))
                    pool.dma_start(x_in[:, r], x1_rows[i]).then_inc(x_landed[r], 16)
                    if i != NB - 1:
                        stored(1, i)
                        pool.wait_ge(turn0_done, NB)
                        if m >= 2:
                            pool.wait_ge(y_t_ready, m - 1)
                        pool.dma_start(sums_in[:, r, :], sums_rows[1, i]).then_inc(x_landed[r], 16)
                elif kind == "store_out":
                    r = third[i] % 2
                    pool.wait_ge(out_ready, third[i] + 1)
                    pool.dma_start(out[i], o[:, r]).then_inc(out_stored[r], 16)
            for r in range(2):
                pool.wait_ge(out_stored[r], 16 * (NB // 2))

        @block.tensor
        def _(pe):
            for u in range(end + 1):
                for kind, i in plan.pe_before.get(u, []):
                    if kind == "features0":
                        if i == 0:
                            pe.wait_ge(const_landed, 32)
                        else:
                            pe.wait_ge(mixed0_used, i)
                        pe.wait_ge(x_t_landed[i % 2], 16 * (i // 2 + 1))
                        for q in range(Q):
                            mm = nc.tensor.matmul(mixed_q[:, q, :], x_t[:, i % 2, q * P:(q + 1) * P], w_sb[:, :],
                                                  start=True, stop=True)
                        mm.then_inc(mixed0_done, 1)

                    elif kind == "degree":
                        if i == 0:
                            pe.wait_ge(consts_ready, 1)
                        pe.wait_ge(row_folded, i + 1)
                        for q in range(Q):
                            mm = nc.tensor.matmul(turned[:, q:q + 1], rowsum[:, q * P:(q + 1) * P], ones[:, :],
                                                  start=True, stop=True)
                        mm.then_inc(degree_done, 1)

                    elif kind == "turn0":
                        if i == NB - 1:
                            pe.wait_ge(ident_ready, 2)
                            pe.wait_ge(deg_ready, NB)
                        else:
                            pe.wait_ge(h_ready, up(i))
                        pe.wait_ge(sums0_ready, up(i) + 1)
                        for q in range(Q):
                            mm = nc.tensor.transpose(turned_q[:, q, :], sums_in[:, up(i) % 2, q * P:(q + 1) * P],
                                                     ident[:, :])
                        mm.then_inc(turn0_done, 1)

                    elif kind == "turn1":
                        if i == NB - 1:
                            pe.wait_ge(mixed0_used, NB)
                        else:
                            pe.wait_ge(feat1_ready, up(i))
                        pe.wait_ge(x1_ready, up(i) + 1)
                        for q in range(Q):
                            mm = nc.tensor.transpose(mixed_q[:, q, :], x1[:, q, :], ident[:, :])
                        mm.then_inc(turn1_done, 1)

                    elif kind == "features1":
                        if i == NB - 1:
                            pe.wait_ge(const1_landed, 32)
                        pe.wait_ge(x1_t_ready, up(i) + 1)
                        for q in range(Q):
                            mm = nc.tensor.matmul(mixed_q[:, q, :], x1_t[:, q * P:(q + 1) * P], w_sb[:, :],
                                                  start=True, stop=True)
                        mm.then_inc(mixed1_done, 1)

                    elif kind == "turn_out":
                        if third[i] == 0:
                            pe.wait_ge(h_ready, NB)
                        else:
                            pe.wait_ge(z_ready, 2 * third[i] - 1)
                        pe.wait_ge(y_t_ready, third[i] + 1)
                        for q in range(Q):
                            mm = nc.tensor.transpose(turned_q[:, q, :], y_t[:, third[i] % 2, q * P:(q + 1) * P],
                                                     ident[:, :])
                        mm.then_inc(turn_out_done, 1)

                if u == end:
                    break
                n, i, j, layers = takes[u]
                for layer in layers:
                    g = plan.group[u][layer]
                    if u == plan.first[g] and plan.bank_turn[g] > 0:
                        pe.wait_ge(bank_emptied[plan.bank[g]], plan.bank_turn[g])
                    if layer == 0:
                        pe.wait_ge(feat0_ready, j + 1)
                    else:
                        pe.wait_ge(feat1_ready, up(j) + 1)
                sums = loads[n][0] == 1 and pe_sums(i, j)
                if sums and j == 0:
                    pe.wait_ge(row_folded, i)
                    if i == 1:
                        pe.wait_ge(consts_ready, 1)
                for half in range(2):
                    a_high, a_low = high(2 * u + half), low(2 * u + half)
                    pe.wait_ge(low_ready, 2 * u + half + 1)
                    if half == 1 and u == plan.last.get(("left1", i)):
                        bank = acc[plan.bank[("left1", i)]]
                        for q in range(Q):
                            for f in (feat_high[1], feat_low[1]):
                                nc.tensor.matmul(bank[:, q * P:(q + 1) * P], f[:, i * Q + q, :], ident_r[:, :],
                                                 start=False, stop=False,
                                                 skip_group_check=True)
                    for layer in layers:
                        g = plan.group[u][layer]
                        for c in range(HQ):
                            q = half * HQ + c
                            chunk = slice(c * T, (c + 1) * T)
                            f_high, f_low = (f[layer][:, j * Q + q, :] for f in (feat_high, feat_low))
                            bank = acc[plan.bank[g]][:, :]
                            nc.tensor.matmul(bank, f_high, a_high[:, chunk], start=(u == plan.first[g] and q == 0), stop=False)
                            nc.tensor.matmul(bank, f_high, a_low[:, chunk], start=False, stop=False)
                            mm = nc.tensor.matmul(bank, f_low, a_high[:, chunk], start=False,
                                                  stop=(u == plan.last[g] and q == Q - 1))
                    if sums:
                        for c in range(HQ):
                            q = half * HQ + c
                            nc.tensor.matmul(part[:, :], ones_r[:, :], a_high[:, c * T:(c + 1) * T],
                                             start=(j == 0 and q == 0), stop=False)
                            mm = nc.tensor.matmul(part[:, :], ones_r[:, :], a_low[:, c * T:(c + 1) * T],
                                                  start=False, stop=(j == PE_SUMS[i] - 1 and q == Q - 1))
                    mm.then_inc(halves_used, 1)

        @block.scalar
        def _(act):
            for kind, i in plan.act:
                if kind == "high":
                    n = takes[i][0]
                    act.wait_ge(tile_landed[plan.slot[n]], 16 * plan.landings[n])
                    for half in range(2):
                        m = 2 * i + half
                        if plan.half_before[m] >= 0:
                            act.wait_ge(halves_used, plan.half_before[m] + 1)
                        nc.scalar.copy(high(m), raw(n)[:, half * HALF:(half + 1) * HALF])\
                            .then_inc(high_ready, 1)
                elif kind == "root":
                    act.wait_ge(deg_ready, i + 1)
                    nc.scalar.activation(root[:, :, :], deg[:, :, :], ACT.Sqrt).then_inc(root_ready, 1)
                elif kind == "features0_high":
                    act.wait_ge(scale_ready, i + 1)
                    for q in range(Q):
                        ins = nc.scalar.activation(feat_high[0][:, i * Q + q, :], biased[:, q, :], ACT.Copy,
                                                   scale=scale[:, i, 0, q:q + 1])
                    ins.then_inc(feat0_high_ready, 1)
                elif kind in ("empty_early0", "empty_right1"):
                    g = (kind[6:], i)
                    b = plan.bank[g]
                    act.wait_ge(halves_used, 2 * plan.last[g] + 2)
                    if (kind, i) in stage_at:
                        m = stage_at[(kind, i)]
                        if m >= 2:
                            act.wait_ge(sums_stored[m % 2], 16 * (m // 2))
                        nc.scalar.copy(stage[:, m % 2, :], acc[b][:, :]).then_inc(bank_emptied[b], 1)
                        act.wait_ge(bank_emptied[b], plan.bank_turn[g] + 1)
                        act.sem_inc(staged, 1)
                    else:
                        if i >= NB - 2:
                            act.wait_ge(scale_ready, NB)
                        else:
                            act.wait_ge(turn0_done, up(i) - 1)
                        nc.scalar.copy(sums_in[:, up(i) % 2, :], acc[b][:, :]).then_inc(bank_emptied[b], 1)
                        act.wait_ge(bank_emptied[b], plan.bank_turn[g] + 1)
                        act.sem_inc(sums0_ready, 1)
                elif kind in ("root_x1", "root_out"):
                    act.wait_ge(var_ready, norm[(kind.replace("root", "make"), i)] + 1)
                    nc.scalar.activation(sdev[:, :], var[:, :], ACT.Sqrt).then_inc(sdev_ready, 1)
                elif kind == "x1_columns":
                    act.wait_ge(turn1_done, up(i) + 1)
                    nc.scalar.copy(x1_t[:, :], mixed[:, :]).then_inc(x1_t_ready, 1)
                elif kind == "features1_high":
                    act.wait_ge(mixed1_done, up(i) + 1)
                    for q in range(Q):
                        ins = nc.scalar.activation(feat_high[1][:, i * Q + q, :], mixed_q[:, q, :], ACT.Copy,
                                                   scale=scale[:, i, 1, q:q + 1])
                    ins.then_inc(feat1_high_ready, 1)

        @block.vector
        def _(dve):
            taken = [0]

            def then(ins):
                taken[0] += 1
                ins.then_inc(dve_step, 1)
                dve.wait_ge(dve_step, taken[0])

            nc.vector.memset(margin[:, 1, :], 0.0)
            nc.vector.memset(margin[:, 0, :], 1e-8)
            nc.vector.memset(ones_r[:, :].bitcast(F32), 1.0)
            nc.vector.memset(ones[:, :], 1.0).then_inc(consts_ready, 1)
            dve.wait_ge(consts_ready, 1)

            def heron(dst, square, guess):
                then(nc.vector.tensor_scalar(guess, guess, 1e-30, None, ALU.max))
                then(nc.vector.reciprocal(dst, guess))
                then(nc.vector.tensor_tensor(dst, dst, square, ALU.mult))
                then(nc.vector.tensor_tensor(dst, dst, guess, ALU.add))

            def moments_of_h():
                for q in range(Q):
                    ins = nc.vector.bn_stats(stats[:, q, :], h[:, q, :])
                then(ins)
                for q in range(Q):
                    ins = nc.vector.bn_aggr(moments[:, q, :], stats[:, q, :])
                then(ins)
                nc.vector.tensor_scalar(var[:, :], moments[:, :, 1], 1e-5, None, ALU.add).then_inc(var_ready, 1)

            def normalise(m, dst, done):
                dve.wait_ge(sdev_ready, m + 1)
                heron(rstd[:, :], var[:, :], sdev[:, :])
                then(nc.vector.tensor_scalar(rstd[:, :], rstd[:, :], 0.5, None, ALU.mult))
                then(nc.vector.reciprocal(rstd[:, :], rstd[:, :]))
                for q in range(Q):
                    ins = nc.vector.tensor_scalar(dst[:, q, :], h[:, q, :], moments[:, q, 0:1], rstd[:, q:q + 1],
                                                  ALU.subtract, ALU.mult)
                ins.then_inc(done, 1)

            in_row = 0
            for kind, i in plan.dve:
                if kind == "low":
                    n = takes[i][0]
                    for half in range(2):
                        m = 2 * i + half
                        dve.wait_ge(high_ready, m + 1)
                        nc.vector.tensor_tensor(low(m), raw(n)[:, half * HALF:(half + 1) * HALF],
                                                high(m).bitcast(F32), ALU.subtract).then_inc(low_ready, 1)

                elif kind == "sum":
                    dve.wait_ge(tile_landed[plan.slot[i]], 16 * plan.landings[i])
                    if in_row == 0:
                        if i >= NB:
                            dve.wait_ge(row_folded, i // NB)
                        ins = nc.vector.tensor_copy(run[:, :], raw(i))
                    else:
                        dve.wait_ge(tile_summed, plan.summed[i] - 1)
                        ins = nc.vector.tensor_tensor(run[:, :], run[:, :], raw(i), ALU.add)
                    ins.then_inc(tile_summed, 1)
                    in_row += 1

                elif kind == "fold":
                    in_row = 0
                    dve.wait_ge(tile_summed, plan.summed[NB * (i + 1) - 1])
                    if i > 0:
                        dve.wait_ge(degree_done, i)
                    ins = nc.vector.tensor_reduce(rowsum[:, :], run[:, :].rearrange("p (q n) -> p n q", q=Q), AX.X,
                                                  ALU.add)
                    if i > 0:
                        then(ins)
                        shared = [u for u, t in enumerate(takes) if loads[t[0]] == (1, i, PE_SUMS[i] - 1)][0]
                        dve.wait_ge(halves_used, 2 * shared + 2)
                        ins = nc.vector.tensor_tensor(rowsum[0:1, :], rowsum[0:1, :], part[0:1, :], ALU.add)
                    ins.then_inc(row_folded, 1)

                elif kind == "take_degree":
                    dve.wait_ge(degree_done, i + 1)
                    if i > 0:
                        dve.wait_ge(root_ready, i)
                        dve.wait_ge(scale_ready, i)
                    nc.vector.tensor_copy(deg[:, 0, :], turned[:, 0:Q])
                    nc.vector.tensor_scalar(deg[:, 1, :], turned[:, 0:Q], 1.0, None, ALU.add).then_inc(deg_ready, 1)

                elif kind == "make_scale":
                    dve.wait_ge(mixed0_done, i + 1)
                    if i > 0:
                        dve.wait_ge(feat0_ready, i)
                    for q in range(Q):
                        ins = nc.vector.tensor_tensor(biased[:, q, :], mixed_q[:, q, :], b_sb[:, :], ALU.add)
                    ins.then_inc(mixed0_used, 1)
                    dve.wait_ge(root_ready, i + 1)
                    heron(inv[:, :, :], deg[:, :, :], root[:, :, :])
                    then(nc.vector.scalar_tensor_tensor(out=inv[:, :, :], in0=inv[:, :, :], scalar=0.5,
                                                        in1=margin[:, :, :], op0=ALU.mult, op1=ALU.add))
                    nc.vector.reciprocal(scale[:, i, :, :], inv[:, :, :]).then_inc(scale_ready, 1)

                elif kind == "features0_low":
                    dve.wait_ge(feat0_high_ready, i + 1)
                    dve.wait_ge(scale_ready, i + 1)
                    for q in range(Q):
                        ins = nc.vector.scalar_tensor_tensor(
                            out=feat_low[0][:, i * Q + q, :], in0=biased[:, q, :], scalar=scale[:, i, 0, q:q + 1],
                            in1=feat_high[0][:, i * Q + q, :].bitcast(F32), op0=ALU.mult, op1=ALU.subtract)
                    ins.then_inc(feat0_ready, 1)

                elif kind == "empty_late0":
                    g = ("late0", i)
                    b, (r, loaded) = plan.bank[g], ring_of_x(i)
                    dve.wait_ge(halves_used, 2 * plan.last[g] + 2)
                    dve.wait_ge(x_landed[r], loaded)
                    nc.vector.tensor_tensor(sums_in[:, r, :], sums_in[:, r, :], acc[b][:, :], ALU.add)\
                        .then_inc(bank_emptied[b], 1)
                    dve.wait_ge(bank_emptied[b], plan.bank_turn[g] + 1)
                    dve.sem_inc(sums0_ready, 1)

                elif kind == "add_x":
                    r, loaded = ring_of_x(i)
                    dve.wait_ge(turn0_done, up(i) + 1)
                    dve.wait_ge(x_landed[r], loaded)
                    if i < NB - 1:
                        dve.wait_ge(x1_ready, up(i))
                    for q in range(Q):
                        ins = nc.vector.scalar_tensor_tensor(
                            out=h[:, q, :], in0=turned_q[:, q, :], scalar=scale[:, i, 0, q:q + 1],
                            in1=x_in[:, r, q, :], op0=ALU.mult, op1=ALU.add)
                    ins.then_inc(h_ready, 1)
                    dve.wait_ge(h_ready, up(i) + 1)
                    moments_of_h()

                elif kind == "make_x1":
                    if i < NB - 1:
                        dve.wait_ge(turn1_done, up(i))
                        dve.wait_ge(x1_stored, 16 * up(i))
                    normalise(norm[(kind, i)], x1, x1_ready)

                elif kind == "features1_low":
                    dve.wait_ge(feat1_high_ready, up(i) + 1)
                    for q in range(Q):
                        ins = nc.vector.scalar_tensor_tensor(
                            out=feat_low[1][:, i * Q + q, :], in0=mixed_q[:, q, :], scalar=scale[:, i, 1, q:q + 1],
                            in1=feat_high[1][:, i * Q + q, :].bitcast(F32), op0=ALU.mult, op1=ALU.subtract)
                    ins.then_inc(feat1_ready, 1)

                elif kind == "empty_left1":
                    g = ("left1", i)
                    b, m, (r, loaded) = plan.bank[g], third[i], ring_of_x1(i)
                    dve.wait_ge(halves_used, 2 * plan.last[g] + 2)
                    if m >= 2:
                        dve.wait_ge(turn_out_done, m - 1)
                    if i == NB - 1:
                        ins = nc.vector.tensor_copy(y_t[:, r, :], acc[b][:, :])
                    else:
                        dve.wait_ge(x_landed[r], loaded)
                        ins = nc.vector.tensor_tensor(y_t[:, r, :], acc[b][:, :], sums_in[:, r, :], ALU.add)
                    ins.then_inc(bank_emptied[b], 1)
                    dve.wait_ge(bank_emptied[b], plan.bank_turn[g] + 1)
                    dve.sem_inc(y_t_ready, 1)

                elif kind == "add_x1":
                    m, (r, loaded) = third[i], ring_of_x1(i)
                    dve.wait_ge(turn_out_done, m + 1)
                    if m == 0:
                        dve.wait_ge(x1_stored, 16 * NB)
                        dve.wait_ge(x1_ready, NB)
                    else:
                        dve.wait_ge(out_ready, m)
                    for q in range(Q):
                        ins = nc.vector.scalar_tensor_tensor(
                            out=z[:, q, :], in0=turned_q[:, q, :], scalar=scale[:, i, 1, q:q + 1],
                            in1=b_sb[:, :], op0=ALU.mult, op1=ALU.add)
                    ins.then_inc(z_ready, 1)
                    dve.wait_ge(z_ready, 2 * m + 1)
                    dve.wait_ge(x_landed[r], loaded)
                    nc.vector.scalar_tensor_tensor(out=h[:, :, :], in0=z[:, :, :], scalar=0.0,
                                                   in1=x_in[:, r], op0=ALU.max, op1=ALU.add).then_inc(z_ready, 1)
                    dve.wait_ge(z_ready, 2 * m + 2)
                    moments_of_h()

                elif kind == "make_out":
                    m = third[i]
                    if m >= 2:
                        dve.wait_ge(out_stored[m % 2], 16 * (m // 2))
                    else:
                        for r in range(2):
                            dve.wait_ge(sums_stored[r], 16 * len([k for k in stage_at.values() if k % 2 == r]))
                    normalise(norm[(kind, i)], o[:, m % 2], out_ready)


def kernel(x, adj, L0_gnn_W, L0_gnn_b, L1_gnn_W, L1_gnn_b):
    import numpy as _np
    import concourse.bacc as _bacc
    from concourse.bass_utils import run_bass_kernel_spmd as _run

    arrays = {
        "x_rows": _np.ascontiguousarray(_np.asarray(x).reshape(NB, Q, P, P).transpose(0, 2, 1, 3)),
        "x_cols": _np.ascontiguousarray(_np.asarray(x).T),
        "adj_tiles": _np.ascontiguousarray(
            _np.asarray(adj).reshape(NB, T, NB, Q, P).transpose(0, 2, 4, 3, 1)).reshape(NB, NB, P, TILE),
        "w0": _np.ascontiguousarray(L0_gnn_W),
        "b0": _np.ascontiguousarray(L0_gnn_b),
        "w1": _np.ascontiguousarray(L1_gnn_W),
        "b1": _np.ascontiguousarray(L1_gnn_b),
    }
    nc = _bacc.Bacc("TRN2", target_bir_lowering=False, num_devices=1)
    args = [nc.dram_tensor(name, a.shape, F32, kind="ExternalInput").ap() for name, a in arrays.items()]
    args.append(nc.dram_tensor("out_rows", (NB, P, Q, P), F32, kind="ExternalOutput").ap())
    args.append(nc.dram_tensor("x1_rows", (NB, P, Q, P), F32, kind="Internal").ap())
    args.append(nc.dram_tensor("sums_rows", (2, NB, P, T), F32, kind="Internal").ap())
    gnn_kernel(nc, *args)
    r = _run(nc, [arrays], core_ids=[0])
    got = r.results[0]["out_rows"]
    return _np.ascontiguousarray(got.transpose(0, 2, 1, 3)).reshape(N, P)
```
